# Optimizing a Trainium2 kernel written in Bass

```python
import numpy as np
import jax
import jax.numpy as jnp

def _softmax(x, axis=-1):
    return jax.nn.softmax(x, axis=axis)

def _gelu(x):
    return jax.nn.gelu(x, approximate=True)

def _silu(x):
    return jax.nn.silu(x)

def _sigmoid(x):
    return jax.nn.sigmoid(x)

def _layernorm(x, axis=-1, eps=1e-05):
    m = jnp.mean(x, axis=axis, keepdims=True)
    v = jnp.var(x, axis=axis, keepdims=True)
    return (x - m) / jnp.sqrt(v + eps)

def _scatter_add(tgt, idx, src, axis=0):
    return tgt.at[idx].add(src)

def _segment_sum(src, seg, n):
    return jax.ops.segment_sum(src, seg, n)
kernel_name = 'mk_conv_preact_d1_conv_nchw256_r2_d849b3'

def setup_inputs(seed: int=0):
    np.random.seed(seed)
    _w = jnp.asarray

    def _rec_inputs():
        import jax
        import jax.numpy as jnp
        _gk = jax.random.key(seed)
        x = -0.0002091 + 1 * jax.random.normal(jax.random.fold_in(_gk, 1), (32, 128, 56, 56), jnp.float32)
        return x
    x = _rec_inputs()

    def _L0_conv_setup():
        import jax, jax.numpy as jnp
        import numpy as np
        THRESHOLD = 0.05

        def _quantize(weight, Wp, Wn):
            max_val = jnp.max(jnp.abs(weight))
            safe_max = jnp.where(max_val > 0, max_val, jnp.ones_like(max_val))
            w_norm = jnp.where(max_val > 0, weight / safe_max, weight)
            delta = THRESHOLD * jnp.max(jnp.abs(w_norm))
            tern = jnp.where(w_norm > delta, 1.0, jnp.where(w_norm < -delta, -1.0, 0.0)).astype(weight.dtype)
            wq = jnp.where(tern > 0, Wp[0] * tern, jnp.where(tern < 0, Wn[0] * tern, tern))
            return wq
        key = jax.random.key(seed)
        k1, k2, k3 = jax.random.split(key, 3)
        x = jax.random.normal(k1, (32, 128, 56, 56), dtype=jnp.float32)
        weight = jax.random.normal(k2, (128, 128, 3, 3), dtype=jnp.float32) * 0.05
        bias = jax.random.normal(k3, (128,), dtype=jnp.float32) * 0.01
        Wp = jnp.ones((1,), dtype=jnp.float32)
        Wn = jnp.ones((1,), dtype=jnp.float32)
        return {'x': x, 'weight': weight, 'bias': bias, 'Wp': Wp, 'Wn': Wn}
    _L0_conv_all = _L0_conv_setup()
    _L0_conv_in = {k: v for k, v in _L0_conv_all.items() if k in ('weight', 'bias', 'Wp', 'Wn')}
    del _L0_conv_all
    return {'x': x, 'L0_conv_weight': _L0_conv_in['weight'], 'L0_conv_bias': _L0_conv_in['bias'], 'L0_conv_Wp': _L0_conv_in['Wp'], 'L0_conv_Wn': _L0_conv_in['Wn']}

def reference(x, L0_conv_weight, L0_conv_bias, L0_conv_Wp, L0_conv_Wn):
    import jax
    import jax.numpy as jnp

    def _L0_conv_ref(x, weight, bias, Wp, Wn):
        import jax, jax.numpy as jnp
        import numpy as np
        THRESHOLD = 0.05

        def _quantize(weight, Wp, Wn):
            max_val = jnp.max(jnp.abs(weight))
            safe_max = jnp.where(max_val > 0, max_val, jnp.ones_like(max_val))
            w_norm = jnp.where(max_val > 0, weight / safe_max, weight)
            delta = THRESHOLD * jnp.max(jnp.abs(w_norm))
            tern = jnp.where(w_norm > delta, 1.0, jnp.where(w_norm < -delta, -1.0, 0.0)).astype(weight.dtype)
            wq = jnp.where(tern > 0, Wp[0] * tern, jnp.where(tern < 0, Wn[0] * tern, tern))
            return wq
        wq = _quantize(weight, Wp, Wn)
        out = jax.lax.conv_general_dilated(x, wq, window_strides=(1, 1), padding=((1, 1), (1, 1)), lhs_dilation=(1, 1), rhs_dilation=(1, 1), dimension_numbers=('NCHW', 'OIHW', 'NCHW'), feature_group_count=1)
        return out + bias[None, :, None, None]

    def _gn(v, G=32, eps=1e-05):
        B_, C_, H_, W_ = v.shape
        g = v.reshape(B_, G, C_ // G, H_, W_)
        m = jnp.mean(g, axis=(2, 3, 4), keepdims=True)
        s = jnp.var(g, axis=(2, 3, 4), keepdims=True)
        return ((g - m) / jnp.sqrt(s + eps)).reshape(v.shape)

    def _ln_c(v, eps=1e-06):
        m = jnp.mean(v, axis=1, keepdims=True)
        s = jnp.var(v, axis=1, keepdims=True)
        return (v - m) / jnp.sqrt(s + eps)

    def _ln_t(v, eps=1e-05):
        m = jnp.mean(v, axis=-1, keepdims=True)
        s = jnp.var(v, axis=-1, keepdims=True)
        return (v - m) / jnp.sqrt(s + eps)

    def _to_tokens(v):
        B_, C_, H_, W_ = v.shape
        return v.reshape(B_, C_, H_ * W_).transpose(0, 2, 1)

    def _from_tokens(t, like):
        B_, C_, H_, W_ = like.shape
        return t.transpose(0, 2, 1).reshape(B_, C_, H_, W_)
    x = x + _L0_conv_ref(_gn(x), L0_conv_weight, L0_conv_bias, L0_conv_Wp, L0_conv_Wn)
    return x

_drawn_inputs = setup_inputs


def setup_inputs(seed=0):
    import zlib

    import numpy as np

    out = dict(_drawn_inputs(seed))
    spreads = {}
    factors = {'L0_conv_bias': 174.019}
    for name, (base, spread) in spreads.items():
        noise = np.random.default_rng([zlib.crc32(name.encode()), seed]).standard_normal(out[name].shape)
        drawn = base * np.exp(spread * noise) if base else spread * noise
        out[name] = jnp.asarray(drawn.astype(out[name].dtype))
    for name, factor in factors.items():
        out[name] = (out[name] * factor).astype(out[name].dtype)
    return out
```

```python
from contextlib import ExitStack

import concourse.bass as bass
from concourse import mybir


P = 128
GROUPS = 32
EPS = 1e-5
THRESHOLD = 0.05
NORM_SCALE = 256.0
X_BUFS = 4
CHUNKS = 4
C, D, A, B = range(4)
HI, LO = range(2)

ALU = mybir.AluOpType
ACT = mybir.ActivationFunctionType
F16 = mybir.dt.float16
F32 = mybir.dt.float32
I32 = mybir.dt.int32
AX_X = mybir.AxisListType.X


def conv_preact_kernel(nc, x, weight, bias, wp, wn, out):
    N_IMG, CH, H, W = x.shape
    TAPS = 3
    PAIRS = H // 2
    ROWS = PAIRS // CHUNKS
    COLS = ROWS * W
    PW = W + 2
    GROUP_N = CH // GROUPS * H * W
    assert CH == P and weight.shape == (P, P, TAPS, TAPS) and PAIRS % CHUNKS == 0
    assert N_IMG % X_BUFS == 0 and COLS <= 512 and N_IMG >= 2 * X_BUFS

    x_dram = x.rearrange("n c h w -> n c (h w)")
    out_dram = out.rearrange("n c h w -> n c (h w)")

    with ExitStack() as ctx:
        def sb(name, shape, dt=F32):
            return ctx.enter_context(nc.sbuf_tensor(name, shape, dt))

        def bank(name):
            return ctx.enter_context(nc.psum_tensor(name, [P, 512], F32))

        def sem(name):
            return ctx.enter_context(nc.semaphore(name))

        x_sb = [sb(f"x{b}", [P, H, W]) for b in range(X_BUFS)]
        normed = [sb(f"normed{b}", [P, H + 2, W]) for b in range(2)]
        plane = [sb(f"plane{j}", [P, PAIRS, W]) for j in range(4)]
        parts = sb("parts", [P, 2, 4, 2, PAIRS, PW], F16)
        c_sb = sb("c_sb", [P, 2, ROWS, W])
        rows_sb = sb("rows_sb", [P, 2, 2, ROWS, W])
        junk = sb("junk", [P, H * W], F16)
        w_raw = sb("w_raw", [P, P, TAPS, TAPS])
        w_norm = sb("w_norm", [P, P, TAPS, TAPS])
        w_pos = sb("w_pos", [P, P, TAPS, TAPS])
        w_neg = sb("w_neg", [P, P, TAPS, TAPS])
        w_sum = sb("w_sum", [P, TAPS, P])
        w_mid = sb("w_mid", [P, TAPS, P])
        w_comb = sb("w_comb", [P, 4, TAPS, P], F16)
        w_lhsT = sb("w_lhsT", [P, 4, TAPS, P], F16)
        ident = sb("ident", [P, P], F16)
        group_mean = sb("group_mean", [P, P])
        w_absmax = sb("w_absmax", [P, 1])
        w_max = sb("w_max", [P, 1])
        w_consts = sb("w_consts", [P, 8])
        bias_sb = sb("bias_sb", [P, 1])
        wp_sb = sb("wp_sb", [P, 1])
        wn_sb = sb("wn_sb", [P, 1])
        equal = sb("equal", [P, 1])
        differ = sb("differ", [1, 1], I32)
        no_bias = sb("no_bias", [P, 1])
        out_scale = sb("out_scale", [P, 2, 2])
        x_sum = sb("x_sum", [P, X_BUFS])
        x_sumsq = sb("x_sumsq", [P, X_BUFS])
        negmean = sb("negmean", [P, X_BUFS])
        var_eps = sb("var_eps", [P, X_BUFS])
        std = sb("std", [P, X_BUFS])
        rstd0 = sb("rstd0", [P, X_BUFS])
        newton = sb("newton", [P, 2, X_BUFS])
        norm_scale = sb("norm_scale", [P, X_BUFS])
        norm_bias = sb("norm_bias", [P, X_BUFS])

        banks = {C: [bank("c0"), bank("c1")], D: [bank("d0"), bank("d1")],
                 A: [bank("a0"), bank("a1")], B: [bank("b0")]}
        stat_ps = bank("stat_ps")

        def product_ps(p, c):
            t = banks[p]
            return t[c % len(t)][:, 0:COLS].rearrange("p (r w) -> p r w", w=W)

        x_loaded = [sem(f"x_loaded{b}") for b in range(X_BUFS)]
        prev_loaded = [sem(f"prev_loaded{b}") for b in range(X_BUFS)]
        y_stored = [sem(f"y_stored{b}") for b in range(X_BUFS)]
        w_loaded = sem("w_loaded")
        scalars_loaded = sem("scalars_loaded")
        consts_step = sem("consts_step")
        consts_ready = sem("consts_ready")
        w_max_local = sem("w_max_local")
        w_max_ready = sem("w_max_ready")
        w_step = sem("w_step")
        flag_ready = sem("flag_ready")
        scale_ready = sem("scale_ready")
        pads_zeroed = sem("pads_zeroed")
        w_comb_ready = sem("w_comb_ready")
        w_turned = sem("w_turned")
        w_ready = sem("w_ready")
        sum_ready = sem("sum_ready")
        mean_summed = sem("mean_summed")
        negmean_ready = sem("negmean_ready")
        sumsq_ready = sem("sumsq_ready")
        var_summed = sem("var_summed")
        var_ready = sem("var_ready")
        std_ready = sem("std_ready")
        stat_step = sem("stat_step")
        affine_ready = sem("affine_ready")
        norm_ready = sem("norm_ready")
        plane_ready = [sem(f"plane_ready{j}") for j in range(4)]
        hi_ready = [sem(f"hi_ready{j}") for j in range(4)]
        lo_ready = [sem(f"lo_ready{j}") for j in range(4)]
        product_done = sem("product_done")
        c_ready = sem("c_ready")
        residual_added = sem("residual_added")
        d_added = sem("d_added")
        even_done = sem("even_done")
        odd_done = sem("odd_done")

        def wait(eng, s, value):
            if not (isinstance(value, int) and value <= 0):
                eng.wait_ge(s, value)

        class Image:

            def __init__(self, q, j):
                self.buf = j % X_BUFS
                self.turn = q + j // X_BUFS
                self.pair = j % 2
                self.q, self.j = q, j

            def count(self, per=1, plus=0):
                return self.q * (per * X_BUFS) + (self.j * per + plus)

            def chunk(self, c, per=1, plus=0):
                return self.count(CHUNKS * per, c * per + plus)

            def two_back(self, c, per=1):
                first = self.j == 0 and c == 0
                return self.chunk(c, per, 0 if first else -per)

        def plane_rows(img, j):
            g = normed[img.pair]
            even, odd = g[:, 0:H:2, :], g[:, 1:H + 1:2, :]
            even2, odd2 = g[:, 2:H + 2:2, :], g[:, 3:H + 2:2, :]
            return {C: (odd, even2, ALU.add), D: (even2, odd, ALU.subtract),
                    A: (even, even2, ALU.subtract), B: (odd, odd2, ALU.subtract)}[j]

        def part(img, j, which):
            return parts[:, img.pair, j, which, :, 1:W + 1]

        def make_plane(wait_eng, eng, img, j):
            wait(wait_eng, norm_ready, img.count(plus=1))
            wait(wait_eng, hi_ready[j], img.count())
            wait(wait_eng, lo_ready[j], img.count())
            a, b, op = plane_rows(img, j)
            eng.tensor_tensor(plane[j][:], a, b, op).then_inc(plane_ready[j], 1)

        def make_lo(wait_eng, eng, img, j):
            wait(wait_eng, hi_ready[j], img.count(plus=1))
            wait(wait_eng, product_done, img.count(16, -16))
            eng.tensor_tensor(part(img, j, LO), plane[j][:], part(img, j, HI),
                              ALU.subtract).then_inc(lo_ready[j], 1)

        def slots(p, eng, emit):
            q0, q1 = p * N_IMG // X_BUFS, (p + 1) * N_IMG // X_BUFS
            emit(q0, -2)
            emit(q0, -1)
            with eng.Fori(q0, q1 - 1) as q:
                for j in range(X_BUFS):
                    emit(q, j)
            for j in range(X_BUFS):
                emit(q1 - 1, j, True)

        def stages(q, j, last):
            now = Image(q, j) if j >= 0 else None
            nxt = Image(q, j + 1) if j >= -1 and not (last and j + 1 >= X_BUFS) else None
            far = Image(q, j + 2) if not (last and j + 2 >= X_BUFS) else None
            return now, nxt, far

        block = ctx.enter_context(nc.Block())

        @block.sync
        def _(sp):
            sp.dma_start(x_sb[0][:].rearrange("p h w -> p (h w)"), x_dram[0]).then_inc(x_loaded[0], 16)
            sp.dma_start(w_raw[:], weight).then_inc(w_loaded, 16)
            sp.dma_start(bias_sb[:], bias.rearrange("(c a) -> c a", a=1)).then_inc(scalars_loaded, 16)
            sp.dma_start(wp_sb[:], wp.rearrange("(a b) -> a b", a=1).broadcast_to([P, 1])).then_inc(scalars_loaded, 16)
            sp.dma_start(wn_sb[:], wn.rearrange("(a b) -> a b", a=1).broadcast_to([P, 1])).then_inc(scalars_loaded, 16)

            def run(p):
                base = p * N_IMG

                def load(img):
                    wait(sp, y_stored[img.buf], img.turn * 16)
                    sp.dma_start(x_sb[img.buf][:].rearrange("p h w -> p (h w)"),
                                 x_dram[img.count(plus=-base)]).then_inc(x_loaded[img.buf], 16)

                def store(img):
                    wait(sp, even_done, img.chunk(CHUNKS))
                    wait(sp, odd_done, img.chunk(CHUNKS))
                    sp.dma_start(out_dram[img.count(plus=-base)],
                                 x_sb[img.buf][:].rearrange("p h w -> p (h w)")).then_inc(y_stored[img.buf], 16)

                def load_first_output(img):
                    wait(sp, norm_ready, img.count(plus=1))
                    sp.dma_start(x_sb[img.buf][:].rearrange("p h w -> p (h w)"),
                                 out_dram[img.count(plus=-base)]).then_inc(prev_loaded[img.buf], 16)

                def emit(q, j, last=False):
                    now, nxt, far = stages(q, j, last)
                    if j == -2 and p:
                        load(far)
                    if j == -2:
                        load(Image(q, 1))
                        load(Image(q, 2))
                    if j >= 0 and not (last and j + 3 >= X_BUFS):
                        load(Image(q, j + 3))
                    if now:
                        store(now)
                    if p and nxt:
                        load_first_output(nxt)

                slots(p, sp, emit)
                for b in range(X_BUFS):
                    sp.wait_ge(y_stored[b], (p + 1) * N_IMG // X_BUFS * 16)

            run(0)
            sp.wait_ge(flag_ready, 1)
            with sp.If(sp.value_load(differ[0:1, 0:1], min_val=0, max_val=1) != 0):
                run(1)

        @block.gpsimd
        def _(pool):
            nc.gpsimd.memset(group_mean[:], -1.0 / GROUP_N).then_inc(consts_step, 1)
            nc.gpsimd.memset(ident[:], 0.0).then_inc(consts_step, 1)
            pool.wait_ge(consts_step, 2)
            per = P // GROUPS
            g = group_mean[:].rearrange("p (g c) -> p g c", c=per)
            nc.gpsimd.affine_select(out=g, in_=g, compare_op=ALU.is_ge, fill=0.0, base=0,
                                    pattern=[[-per, GROUPS], [0, per]], channel_multiplier=1).then_inc(consts_step, 1)
            nc.gpsimd.affine_select(out=ident[:], in_=ident[:], compare_op=ALU.not_equal, fill=1.0, base=0,
                                    pattern=[[-1, P]], channel_multiplier=1).then_inc(consts_ready, 1)
            pool.wait_ge(consts_step, 3)
            nc.gpsimd.affine_select(out=g, in_=g, compare_op=ALU.is_ge, fill=0.0, base=per - 1,
                                    pattern=[[per, GROUPS], [0, per]], channel_multiplier=-1).then_inc(consts_ready, 1)
            pool.wait_ge(w_max_local, 1)
            nc.gpsimd.partition_all_reduce(w_max[:], w_absmax[:], P, bass.bass_isa.ReduceOp.max).then_inc(w_max_ready, 1)

            def run(p):
                def add_residual(img, c):
                    pool.wait_ge(c_ready, img.chunk(c, 1, 1))
                    wait(pool, even_done, img.two_back(c))
                    wait(pool, odd_done, img.two_back(c))
                    if p:
                        pool.wait_ge(prev_loaded[img.buf], (img.turn - N_IMG // X_BUFS) * 16 + 16)
                    for odd in range(2):
                        first = 2 * ROWS * c + odd
                        nc.gpsimd.tensor_tensor(rows_sb[:, c % 2, odd], x_sb[img.buf][:, first:first + 2 * ROWS - 1:2, :],
                                                c_sb[:, c % 2], ALU.add).then_inc(residual_added, 1)

                def emit(q, j, last=False):
                    now, nxt, far = stages(q, j, last)
                    if nxt:
                        make_plane(pool, nc.gpsimd, nxt, A)
                    if now:
                        add_residual(now, 0)
                    if nxt:
                        make_plane(pool, nc.gpsimd, nxt, B)
                    if now:
                        add_residual(now, 1)
                        add_residual(now, 2)
                    if nxt:
                        make_lo(pool, nc.gpsimd, nxt, B)
                    if now:
                        add_residual(now, 3)

                slots(p, pool, emit)

            pool.wait_ge(pads_zeroed, 2)
            run(0)
            pool.wait_ge(flag_ready, 1)
            with pool.If(pool.value_load(differ[0:1, 0:1], min_val=0, max_val=1) != 0):
                run(1)

        @block.scalar
        def _(act):
            def run(p):
                for j in range(4):
                    act.wait_ge(w_turned, 4 * p + j + 1)
                    wait(act, product_done, p * N_IMG * 16)
                    nc.scalar.activation(w_lhsT[:, j].rearrange("p k c -> p (k c)"), banks[j][0][:, 0:TAPS * P],
                                         ACT.Copy).then_inc(w_ready, 1)
                if p == 0:
                    act.wait_ge(scale_ready, 1)
                    act.wait_ge(scalars_loaded, 48)

                def copy_c(img, c):
                    act.wait_ge(product_done, img.chunk(c, 4, C + 1))
                    wait(act, residual_added, img.two_back(c, 2))
                    nc.scalar.activation(c_sb[:, c % 2], product_ps(C, c), ACT.Identity,
                                         bias=(no_bias if p else bias_sb)[:, 0:1],
                                         scale=out_scale[:, p, 0:1]).then_inc(c_ready, 1)

                def make_hi(img, j):
                    act.wait_ge(plane_ready[j], img.count(plus=1))
                    wait(act, product_done, img.count(16, -16))
                    nc.scalar.activation(part(img, j, HI), plane[j][:], ACT.Copy).then_inc(hi_ready[j], 1)

                def sum_x(img):
                    act.wait_ge(x_loaded[img.buf], img.turn * 16 + 16)
                    nc.scalar.activation(junk[:], x_sb[img.buf][:].rearrange("p h w -> p (h w)"), ACT.Copy,
                                         accum_out=x_sum[:, img.buf:img.buf + 1]).then_inc(sum_ready, 1)

                def sum_squares(img):
                    act.wait_ge(negmean_ready, img.count(plus=1))
                    nc.scalar.activation(junk[:], x_sb[img.buf][:].rearrange("p h w -> p (h w)"), ACT.Square,
                                         bias=negmean[:, img.buf:img.buf + 1],
                                         accum_out=x_sumsq[:, img.buf:img.buf + 1]).then_inc(sumsq_ready, 1)

                def root(img):
                    act.wait_ge(var_ready, img.count(plus=1))
                    b = slice(img.buf, img.buf + 1)
                    nc.scalar.activation(std[:, b], var_eps[:, b], ACT.Sqrt).then_inc(std_ready, 1)

                def normalise(img):
                    act.wait_ge(affine_ready, img.count(plus=1))
                    for j in range(4):
                        wait(act, plane_ready[j], img.count(plus=-1))
                    b = slice(img.buf, img.buf + 1)
                    nc.scalar.activation(normed[img.pair][:, 1:H + 1, :], x_sb[img.buf][:], ACT.Identity,
                                         bias=norm_bias[:, b], scale=norm_scale[:, b]).then_inc(norm_ready, 1)

                def emit(q, j, last=False):
                    now, nxt, far = stages(q, j, last)
                    if far:
                        sum_x(far)
                    if now:
                        copy_c(now, 0)
                    if nxt:
                        make_hi(nxt, C)
                        make_hi(nxt, D)
                    if now:
                        copy_c(now, 1)
                    if far:
                        sum_squares(far)
                    if nxt:
                        make_hi(nxt, A)
                    if now:
                        copy_c(now, 2)
                    if nxt:
                        make_hi(nxt, B)
                    if far:
                        root(far)
                    if now:
                        copy_c(now, 3)
                    if far:
                        normalise(far)

                slots(p, act, emit)

            act.wait_ge(pads_zeroed, 2)
            run(0)
            act.wait_ge(flag_ready, 1)
            with act.If(act.value_load(differ[0:1, 0:1], min_val=0, max_val=1) != 0):
                run(1)

        @block.vector
        def _(dve):
            for b in range(2):
                nc.vector.memset(normed[b][:, 0:H + 2:H + 1, :], 0.0)
            nc.vector.memset(no_bias[:], 0.0).then_inc(pads_zeroed, 1)
            nc.vector.memset(parts[:].rearrange("p b j s r w -> p (b j s r) w")[:, :, 0:PW:PW - 1], 0.0).then_inc(pads_zeroed, 1)

            steps = [0]

            def step(ins):
                steps[0] += 1
                ins.then_inc(w_step, 1)
                dve.wait_ge(w_step, steps[0])

            dve.wait_ge(w_loaded, 16)
            raw = w_raw[:].rearrange("p c h w -> p (c h w)")
            nrm = w_norm[:].rearrange("p c h w -> p (c h w)")
            pos = w_pos[:].rearrange("p c h w -> p (c h w)")
            neg = w_neg[:].rearrange("p c h w -> p (c h w)")
            nc.vector.tensor_reduce(w_absmax[:], raw, AX_X, ALU.max, apply_absolute_value=True).then_inc(w_max_local, 1)
            dve.wait_ge(scalars_loaded, 48)
            nc.vector.tensor_tensor(differ[:], wp_sb[0:1, :], wn_sb[0:1, :], ALU.not_equal).then_inc(flag_ready, 1)
            nc.vector.tensor_scalar(out_scale[:, 0, 0:1], wp_sb[:], 1.0 / NORM_SCALE, None, ALU.mult)
            nc.vector.tensor_scalar(out_scale[:, 0, 1:2], wp_sb[:], -1.0 / NORM_SCALE, None, ALU.mult)
            nc.vector.tensor_scalar(out_scale[:, 1, 0:1], wn_sb[:], -1.0 / NORM_SCALE, None, ALU.mult)
            nc.vector.tensor_scalar(out_scale[:, 1, 1:2], wn_sb[:], 1.0 / NORM_SCALE, None, ALU.mult).then_inc(scale_ready, 1)
            nc.vector.tensor_tensor(equal[:], wp_sb[:], wn_sb[:], ALU.is_equal)
            dve.wait_ge(w_max_ready, 1)
            col = [w_consts[:, i:i + 1] for i in range(6)]
            step(nc.vector.tensor_scalar(col[0], w_max[:], 0.0, None, ALU.is_equal))
            step(nc.vector.tensor_tensor(col[1], w_max[:], col[0], ALU.add))
            step(nc.vector.reciprocal(col[2], col[1]))
            nc.vector.tensor_scalar(nrm, raw, col[2], None, ALU.mult)
            step(nc.vector.tensor_scalar(col[3], w_max[:], col[2], THRESHOLD, ALU.mult, ALU.mult))
            step(nc.vector.tensor_scalar(col[4], col[3], -1.0, None, ALU.mult))
            step(nc.vector.tensor_scalar(neg, nrm, col[4], equal[:], ALU.is_lt, ALU.mult))
            step(nc.vector.scalar_tensor_tensor(pos, nrm, col[3], neg, ALU.is_gt, ALU.subtract))
            nc.vector.tensor_scalar(neg, nrm, col[4], None, ALU.is_lt)

            def combine(p):
                w = [(w_neg if p else w_pos)[:, :, kh, :].rearrange("p c k -> p k c") for kh in range(TAPS)]
                wait(dve, w_turned, 4 * p)
                step(nc.vector.tensor_tensor(w_sum[:], w[0], w[2], ALU.add))
                step(nc.vector.tensor_scalar(w_sum[:], w_sum[:], 0.5, None, ALU.mult))
                step(nc.vector.tensor_scalar(w_mid[:], w[1], 0.5, None, ALU.mult))
                nc.vector.tensor_tensor(w_comb[:, C], w_sum[:], w_mid[:], ALU.add)
                nc.vector.tensor_tensor(w_comb[:, D], w_sum[:], w_mid[:], ALU.subtract)
                nc.vector.tensor_scalar(w_comb[:, A], w[0], 1.0, None, ALU.mult)
                nc.vector.tensor_scalar(w_comb[:, B], w[2], -1.0, None, ALU.mult).then_inc(w_comb_ready, 1)

            def run(p):
                def negate_mean(img):
                    dve.wait_ge(mean_summed, img.count(plus=1))
                    b = slice(img.buf, img.buf + 1)
                    nc.vector.tensor_copy(negmean[:, b], stat_ps[:, 0:1]).then_inc(negmean_ready, 1)

                def variance(img):
                    dve.wait_ge(var_summed, img.count(plus=1))
                    b = slice(img.buf, img.buf + 1)
                    nc.vector.tensor_scalar(var_eps[:, b], stat_ps[:, 1:2], -1.0, EPS,
                                            ALU.mult, ALU.add).then_inc(var_ready, 1)

                def affine(img):
                    b = slice(img.buf, img.buf + 1)
                    dve.wait_ge(std_ready, img.count(plus=1))
                    nc.vector.reciprocal(rstd0[:, b], std[:, b]).then_inc(stat_step, 1)
                    dve.wait_ge(stat_step, img.count(4, 1))
                    nc.vector.tensor_scalar(newton[:, 0, b], rstd0[:, b], rstd0[:, b], var_eps[:, b],
                                            ALU.mult, ALU.mult).then_inc(stat_step, 1)
                    dve.wait_ge(stat_step, img.count(4, 2))
                    nc.vector.tensor_scalar(newton[:, 1, b], newton[:, 0, b], -0.5 * NORM_SCALE, 1.5 * NORM_SCALE,
                                            ALU.mult, ALU.add).then_inc(stat_step, 1)
                    dve.wait_ge(stat_step, img.count(4, 3))
                    nc.vector.tensor_tensor(norm_scale[:, b], rstd0[:, b], newton[:, 1, b], ALU.mult).then_inc(stat_step, 1)
                    dve.wait_ge(stat_step, img.count(4, 4))
                    nc.vector.tensor_tensor(norm_bias[:, b], negmean[:, b], norm_scale[:, b], ALU.mult).then_inc(affine_ready, 1)

                def finish_chunk(img, c):
                    dve.wait_ge(product_done, img.chunk(c, 4, D + 1))
                    for odd in range(2):
                        dve.wait_ge(residual_added, img.chunk(c, 2, odd + 1))
                        nc.vector.scalar_tensor_tensor(rows_sb[:, c % 2, odd], product_ps(D, c), out_scale[:, p, odd:odd + 1],
                                                       rows_sb[:, c % 2, odd], ALU.mult, ALU.add).then_inc(d_added, 1)
                    for odd, prod, done in ((0, A, even_done), (1, B, odd_done)):
                        first = 2 * ROWS * c + odd
                        dve.wait_ge(product_done, img.chunk(c, 4, prod + 1))
                        dve.wait_ge(d_added, img.chunk(c, 2, odd + 1))
                        nc.vector.scalar_tensor_tensor(x_sb[img.buf][:, first:first + 2 * ROWS - 1:2, :],
                                                       product_ps(prod, c), out_scale[:, p, 0:1],
                                                       rows_sb[:, c % 2, odd], ALU.mult, ALU.add).then_inc(done, 1)

                def emit(q, j, last=False):
                    now, nxt, far = stages(q, j, last)
                    if nxt:
                        make_plane(dve, nc.vector, nxt, C)
                        make_plane(dve, nc.vector, nxt, D)
                    if now:
                        finish_chunk(now, 0)
                    if far:
                        negate_mean(far)
                    if nxt:
                        make_lo(dve, nc.vector, nxt, C)
                        make_lo(dve, nc.vector, nxt, D)
                    if now:
                        finish_chunk(now, 1)
                    if far:
                        variance(far)
                    if nxt:
                        make_lo(dve, nc.vector, nxt, A)
                    if now:
                        finish_chunk(now, 2)
                    if far:
                        affine(far)
                    if now:
                        finish_chunk(now, 3)

                slots(p, dve, emit)

            combine(0)
            run(0)
            with dve.If(dve.value_load(differ[0:1, 0:1], min_val=0, max_val=1) != 0):
                combine(1)
                run(1)

        @block.tensor
        def _(pe):
            def turn_weights(p):
                pe.wait_ge(consts_ready, 2)
                pe.wait_ge(w_comb_ready, p + 1)
                for s, per in ((c_ready, 1), (d_added, 2), (even_done, 1), (odd_done, 1)):
                    wait(pe, s, p * N_IMG * CHUNKS * per)
                for j in range(4):
                    for kw in range(TAPS):
                        ins = nc.tensor.matmul(banks[j][0][:, kw * P:(kw + 1) * P], w_comb[:, j, kw, :], ident[:],
                                               start=True, stop=True)
                    ins.then_inc(w_turned, 1)

            def run(p):
                def sum_groups(img, of, ready, col, done):
                    pe.wait_ge(ready, img.count(plus=1))
                    wait(pe, var_ready, img.count())
                    nc.tensor.matmul(stat_ps[:, col:col + 1], group_mean[:], of[:, img.buf:img.buf + 1],
                                     start=True, stop=True).then_inc(done, 1)

                def multiply(img, c, prod):
                    if c == 0:
                        pe.wait_ge(hi_ready[prod], img.count(plus=1))
                        pe.wait_ge(lo_ready[prod], img.count(plus=1))
                    if prod == C:
                        wait(pe, c_ready, img.two_back(c))
                    if prod == D:
                        wait(pe, d_added, img.two_back(c, 2))
                    if prod == A:
                        wait(pe, even_done, img.two_back(c))
                    if prod == B:
                        wait(pe, odd_done, img.chunk(c))
                    last = (TAPS - 1, LO)
                    for kw in range(TAPS):
                        for which in (HI, LO):
                            ins = nc.tensor.matmul(product_ps(prod, c), w_lhsT[:, prod, kw, :],
                                                   parts[:, img.pair, prod, which, c * ROWS:(c + 1) * ROWS, kw:kw + W],
                                                   start=(kw, which) == (0, HI), stop=(kw, which) == last)
                    ins.then_inc(product_done, 1)

                def emit(q, j, last=False):
                    now, nxt, far = stages(q, j, last)
                    if j == 0 and isinstance(q, int) and not last:
                        pass
                    for c in range(CHUNKS):
                        if now:
                            for prod in (C, D, A, B):
                                multiply(now, c, prod)
                        if far and c == 0:
                            sum_groups(far, x_sum, sum_ready, 0, mean_summed)
                        if far and c == 2:
                            sum_groups(far, x_sumsq, sumsq_ready, 1, var_summed)

                slots(p, pe, emit)

            turn_weights(0)
            pe.wait_ge(w_ready, 4)
            pe.wait_ge(pads_zeroed, 2)
            run(0)
            pe.wait_ge(flag_ready, 1)
            with pe.If(pe.value_load(differ[0:1, 0:1], min_val=0, max_val=1) != 0):
                turn_weights(1)
                pe.wait_ge(w_ready, 8)
                run(1)


_INS = ['x', 'L0_conv_weight', 'L0_conv_bias', 'L0_conv_Wp', 'L0_conv_Wn']


def kernel(**inputs):
    import numpy as _np
    import concourse.bacc as _bacc
    from concourse import mybir as _mybir
    from concourse.bass_utils import run_bass_kernel_spmd as _run

    nc = _bacc.Bacc("TRN2", target_bir_lowering=False, num_devices=1)
    arrays, args = {}, []
    for name in _INS:
        a = _np.ascontiguousarray(inputs[name])
        arrays[f"in_{name}_dram"] = a
        args.append(nc.dram_tensor(f"in_{name}_dram", a.shape, _mybir.dt.from_np(a.dtype), kind="ExternalInput").ap())
    shape = inputs['x'].shape
    args.append(nc.dram_tensor("out_0_dram", shape, _mybir.dt.float32, kind="ExternalOutput").ap())
    conv_preact_kernel(nc, *args)
    r = _run(nc, [arrays], core_ids=[0])
    return r.results[0]["out_0_dram"]
```

```python
from contextlib import ExitStack

import concourse.bass as bass
from concourse import mybir


P = 128
GROUPS = 32
EPS = 1e-5
THRESHOLD = 0.05
NORM_SCALE = 256.0
X_BUFS = 4
HALVES = 2
C, D, A, B = range(4)
HI, LO = range(2)
PSUM_BANK = 512

ALU = mybir.AluOpType
ACT = mybir.ActivationFunctionType
F16 = mybir.dt.float16
F32 = mybir.dt.float32
I32 = mybir.dt.int32
AX_X = mybir.AxisListType.X


def conv_preact_kernel(nc, x, weight, bias, wp, wn, out):
    N_IMG, CH, H, W = x.shape
    TAPS = 3
    PAIRS = H // 2
    ROWS = PAIRS // HALVES
    COLS = ROWS * W
    ROWS0 = PSUM_BANK // W
    PW = W + 2
    GROUP_N = CH // GROUPS * H * W
    assert CH == P and weight.shape == (P, P, TAPS, TAPS) and PAIRS % HALVES == 0
    assert N_IMG % X_BUFS == 0 and N_IMG >= 3 * X_BUFS
    assert ROWS0 < ROWS and (ROWS - ROWS0) * W < PSUM_BANK - 2

    x_dram = x.rearrange("n c h w -> n c (h w)")
    out_dram = out.rearrange("n c h w -> n c (h w)")

    with ExitStack() as ctx:
        def sb(name, shape, dt=F32):
            return ctx.enter_context(nc.sbuf_tensor(name, shape, dt))

        def sem(name):
            return ctx.enter_context(nc.semaphore(name))

        x_sb = [sb(f"x{b}", [P, H, W]) for b in range(X_BUFS)]
        plane = [[sb(f"plane{b}_{j}", [P, PAIRS, W]) for j in range(4)] for b in range(2)]
        parts = sb("parts", [P, 2, 4, 2, PAIRS, PW], F16)
        c_sb = sb("c_sb", [P, HALVES, ROWS, W])
        rows_sb = sb("rows_sb", [P, HALVES, 2, ROWS, W])
        junk = sb("junk", [P, H * W], F16)
        w_raw = sb("w_raw", [P, P, TAPS, TAPS])
        w_norm = sb("w_norm", [P, P, TAPS, TAPS])
        w_pos = sb("w_pos", [P, P, TAPS, TAPS])
        w_neg = sb("w_neg", [P, P, TAPS, TAPS])
        w_sum = sb("w_sum", [P, TAPS, P])
        w_mid = sb("w_mid", [P, TAPS, P])
        w_comb = sb("w_comb", [P, 4, TAPS, P], F16)
        w_lhsT = sb("w_lhsT", [P, 4, TAPS, P], F16)
        ident = sb("ident", [P, P], F16)
        group_mean = sb("group_mean", [P, P])
        w_absmax = sb("w_absmax", [P, 1])
        w_max = sb("w_max", [P, 1])
        w_consts = sb("w_consts", [P, 8])
        bias_sb = sb("bias_sb", [P, 1])
        wp_sb = sb("wp_sb", [P, 1])
        wn_sb = sb("wn_sb", [P, 1])
        equal = sb("equal", [P, 1])
        differ = sb("differ", [1, 1], I32)
        no_bias = sb("no_bias", [P, 1])
        out_scale = sb("out_scale", [P, 2, 2])
        x_sum = sb("x_sum", [P, X_BUFS])
        x_sumsq = sb("x_sumsq", [P, X_BUFS])
        negmean = sb("negmean", [P, X_BUFS])
        neg2mean = sb("neg2mean", [P, X_BUFS])
        var_eps = sb("var_eps", [P, X_BUFS])
        std = sb("std", [P, X_BUFS])
        rstd0 = sb("rstd0", [P, X_BUFS])
        newton = sb("newton", [P, 2, X_BUFS])
        norm_scale = sb("norm_scale", [P, X_BUFS])

        product = [ctx.enter_context(nc.psum_tensor(f"product{j}", [P, 2 * PSUM_BANK], F32)) for j in range(4)]
        FIRST_COL = PSUM_BANK - ROWS0 * W
        stat_ps = product[C][:, 2 * PSUM_BANK - 2:2 * PSUM_BANK]

        def product_ps(j, r0=0, r1=ROWS):
            return product[j][:, FIRST_COL + r0 * W:FIRST_COL + r1 * W].rearrange("p (r w) -> p r w", w=W)

        x_loaded = [sem(f"x_loaded{b}") for b in range(X_BUFS)]
        prev_loaded = [sem(f"prev_loaded{b}") for b in range(X_BUFS)]
        y_stored = [[sem(f"y_stored{b}_{h}") for h in range(HALVES)] for b in range(X_BUFS)]
        w_loaded = sem("w_loaded")
        scalars_loaded = sem("scalars_loaded")
        consts_step = sem("consts_step")
        consts_ready = sem("consts_ready")
        w_max_local = sem("w_max_local")
        w_max_ready = sem("w_max_ready")
        w_step = sem("w_step")
        flag_ready = sem("flag_ready")
        scale_ready = sem("scale_ready")
        pads_zeroed = sem("pads_zeroed")
        w_comb_ready = sem("w_comb_ready")
        w_turned = sem("w_turned")
        w_ready = sem("w_ready")
        sum_ready = sem("sum_ready")
        mean_summed = sem("mean_summed")
        negmean_ready = sem("negmean_ready")
        sumsq_ready = sem("sumsq_ready")
        var_summed = sem("var_summed")
        var_ready = sem("var_ready")
        std_ready = sem("std_ready")
        stat_step = sem("stat_step")
        scale_of_x_ready = sem("scale_of_x_ready")
        edges_ready = sem("edges_ready")
        plane_ready = [sem(f"plane_ready{j}") for j in range(4)]
        hi_ready = [sem(f"hi_ready{j}") for j in range(4)]
        lo_ready = [sem(f"lo_ready{j}") for j in range(4)]
        product_done = sem("product_done")
        c_ready = sem("c_ready")
        residual_added = sem("residual_added")
        d_added = sem("d_added")
        even_done = sem("even_done")
        odd_done = sem("odd_done")

        def wait(eng, s, value):
            if not (isinstance(value, int) and value <= 0):
                eng.wait_ge(s, value)

        class Image:

            def __init__(self, q, j):
                self.buf = j % X_BUFS
                self.turn = q + j // X_BUFS
                self.pair = j % 2
                self.q, self.j = q, j

            def count(self, per=1, plus=0):
                return self.q * (per * X_BUFS) + (self.j * per + plus)

            def half(self, h, per=1, plus=0):
                return self.count(HALVES * per, h * per + plus)

        def slots(p, eng, emit):
            q0 = p * N_IMG // X_BUFS

            def edge_slot(k):
                emit(*[Image(q0, k + d) if 0 <= k + d < N_IMG else None for d in range(-1, 4)])

            for k in range(-2, 1):
                edge_slot(k)
            with eng.Fori(q0, q0 + N_IMG // X_BUFS - 1) as q:
                for j in range(1, X_BUFS + 1):
                    emit(*[Image(q, j + d) for d in range(-1, 4)])
            for k in range(N_IMG - X_BUFS + 1, N_IMG + 1):
                edge_slot(k)

        def b_slice(img):
            return slice(img.buf, img.buf + 1)

        def part(img, j, which):
            return parts[:, img.pair, j, which, :, 1:W + 1]

        block = ctx.enter_context(nc.Block())

        @block.sync
        def _(sp):
            sp.dma_start(w_raw[:], weight).then_inc(w_loaded, 16)
            sp.dma_start(bias_sb[:], bias.rearrange("(c a) -> c a", a=1)).then_inc(scalars_loaded, 16)
            sp.dma_start(wp_sb[:], wp.rearrange("(a b) -> a b", a=1).broadcast_to([P, 1])).then_inc(scalars_loaded, 16)
            sp.dma_start(wn_sb[:], wn.rearrange("(a b) -> a b", a=1).broadcast_to([P, 1])).then_inc(scalars_loaded, 16)

            def run(p):
                def half_of(img, h):
                    return x_sb[img.buf][:, 2 * ROWS * h:2 * ROWS * (h + 1), :].rearrange("p h w -> p (h w)")

                def in_dram(t, img, h):
                    return t[img.count(plus=-p * N_IMG)][:, h * 2 * COLS:(h + 1) * 2 * COLS]

                def load(img):
                    for h in range(HALVES):
                        wait(sp, y_stored[img.buf][h], img.turn * 16)
                        sp.dma_start(half_of(img, h), in_dram(x_dram, img, h)).then_inc(x_loaded[img.buf], 16)

                def store(img, h):
                    sp.wait_ge(even_done, img.half(h, 1, 1))
                    sp.wait_ge(odd_done, img.half(h, 1, 1))
                    sp.dma_start(in_dram(out_dram, img, h), half_of(img, h)).then_inc(y_stored[img.buf][h], 16)

                def load_first_output(img):
                    for s in plane_ready + [edges_ready, sumsq_ready]:
                        sp.wait_ge(s, img.count(plus=1))
                    for h in range(HALVES):
                        sp.dma_start(half_of(img, h), in_dram(out_dram, img, h)).then_inc(prev_loaded[img.buf], 16)

                def emit(prev, now, nxt, far, ahead):
                    if far and not nxt:
                        load(far)
                    if prev:
                        store(prev, 1)
                    if ahead:
                        load(ahead)
                    if now:
                        store(now, 0)
                    if p and nxt:
                        load_first_output(nxt)

                slots(p, sp, emit)
                for b in range(X_BUFS):
                    for h in range(HALVES):
                        sp.wait_ge(y_stored[b][h], (p + 1) * N_IMG // X_BUFS * 16)

            run(0)
            sp.wait_ge(flag_ready, 1)
            with sp.If(sp.value_load(differ[0:1, 0:1], min_val=0, max_val=1) != 0):
                run(1)

        @block.gpsimd
        def _(pool):
            nc.gpsimd.memset(group_mean[:], -1.0 / GROUP_N).then_inc(consts_step, 1)
            nc.gpsimd.memset(ident[:], 0.0).then_inc(consts_step, 1)
            pool.wait_ge(consts_step, 2)
            per = P // GROUPS
            g = group_mean[:].rearrange("p (g c) -> p g c", c=per)
            nc.gpsimd.affine_select(out=g, in_=g, compare_op=ALU.is_ge, fill=0.0, base=0,
                                    pattern=[[-per, GROUPS], [0, per]], channel_multiplier=1).then_inc(consts_step, 1)
            nc.gpsimd.affine_select(out=ident[:], in_=ident[:], compare_op=ALU.not_equal, fill=1.0, base=0,
                                    pattern=[[-1, P]], channel_multiplier=1).then_inc(consts_ready, 1)
            pool.wait_ge(consts_step, 3)
            nc.gpsimd.affine_select(out=g, in_=g, compare_op=ALU.is_ge, fill=0.0, base=per - 1,
                                    pattern=[[per, GROUPS], [0, per]], channel_multiplier=-1).then_inc(consts_ready, 1)
            pool.wait_ge(w_max_local, 1)
            nc.gpsimd.partition_all_reduce(w_max[:], w_absmax[:], P, bass.bass_isa.ReduceOp.max).then_inc(w_max_ready, 1)

            def run(p):
                def difference(img, j):
                    pool.wait_ge(x_loaded[img.buf], img.turn * 32 + 32)
                    wait(pool, lo_ready[j], img.count(plus=-1))
                    xs, u = x_sb[img.buf], plane[img.pair][j]
                    even, odd = xs[:, 0:H:2, :], xs[:, 1:H:2, :]
                    o, a, b = {D: (u[:], odd, even),
                               A: (u[:, 1:, :], odd[:, 0:PAIRS - 1, :], odd[:, 1:, :]),
                               B: (u[:, 0:PAIRS - 1, :], even[:, 0:PAIRS - 1, :], even[:, 1:, :])}[j]
                    nc.gpsimd.tensor_tensor(o, a, b, ALU.subtract).then_inc(plane_ready[j], 1)

                def add_residual(img, h):
                    pool.wait_ge(c_ready, img.half(h, 1, 1))
                    wait(pool, even_done, img.half(h, 1, -1))
                    wait(pool, odd_done, img.half(h, 1, -1))
                    if p:
                        pool.wait_ge(prev_loaded[img.buf], (img.turn - N_IMG // X_BUFS) * 32 + 32)
                    for odd in range(2):
                        first = 2 * ROWS * h + odd
                        nc.gpsimd.tensor_tensor(rows_sb[:, h, odd], x_sb[img.buf][:, first:first + 2 * ROWS - 1:2, :],
                                                c_sb[:, h], ALU.add).then_inc(residual_added, 1)

                def emit(prev, now, nxt, far, ahead):
                    if now:
                        add_residual(now, 0)
                    if far:
                        difference(far, D)
                        difference(far, A)
                    if now:
                        add_residual(now, 1)
                    if far:
                        difference(far, B)

                slots(p, pool, emit)

            run(0)
            pool.wait_ge(flag_ready, 1)
            with pool.If(pool.value_load(differ[0:1, 0:1], min_val=0, max_val=1) != 0):
                run(1)

        @block.scalar
        def _(act):
            def run(p):
                def turned_weights():
                    wait(act, product_done, p * N_IMG * HALVES * 4)
                    for j in range(4):
                        act.wait_ge(w_turned, 4 * p + j + 1)
                        nc.scalar.activation(w_lhsT[:, j].rearrange("p k c -> p (k c)"), product[j][:, 0:TAPS * P],
                                             ACT.Copy).then_inc(w_ready, 1)

                def copy_c(img, h):
                    if p == 0:
                        act.wait_ge(scale_ready, 1)
                        act.wait_ge(scalars_loaded, 48)
                    act.wait_ge(product_done, img.half(h, 4, C + 1))
                    wait(act, residual_added, img.half(h, 2, -2))
                    nc.scalar.activation(c_sb[:, h], product_ps(C), ACT.Identity,
                                         bias=(no_bias if p else bias_sb)[:, 0:1],
                                         scale=out_scale[:, p, 0:1]).then_inc(c_ready, 1)

                def make_hi(img, j):
                    act.wait_ge(scale_of_x_ready, img.count(plus=1))
                    act.wait_ge(plane_ready[j], img.count(plus=1))
                    if j in (A, B):
                        act.wait_ge(edges_ready, img.count(plus=1))
                    wait(act, product_done, img.count(4 * HALVES, -4 * HALVES))
                    nc.scalar.activation(part(img, j, HI), plane[img.pair][j][:], ACT.Copy,
                                         scale=norm_scale[:, b_slice(img)]).then_inc(hi_ready[j], 1)

                def sum_x(img):
                    act.wait_ge(x_loaded[img.buf], img.turn * 32 + 32)
                    nc.scalar.activation(junk[:], x_sb[img.buf][:].rearrange("p h w -> p (h w)"), ACT.Copy,
                                         accum_out=x_sum[:, b_slice(img)]).then_inc(sum_ready, 1)

                def sum_squares(img):
                    act.wait_ge(negmean_ready, img.count(plus=1))
                    nc.scalar.activation(junk[:], x_sb[img.buf][:].rearrange("p h w -> p (h w)"), ACT.Square,
                                         bias=negmean[:, b_slice(img)],
                                         accum_out=x_sumsq[:, b_slice(img)]).then_inc(sumsq_ready, 1)

                def root(img):
                    act.wait_ge(var_ready, img.count(plus=1))
                    nc.scalar.activation(std[:, b_slice(img)], var_eps[:, b_slice(img)], ACT.Sqrt).then_inc(std_ready, 1)

                def emit(prev, now, nxt, far, ahead):
                    if far and not nxt:
                        turned_weights()
                    if nxt:
                        make_hi(nxt, C)
                    if now:
                        copy_c(now, 0)
                    if far:
                        sum_x(far)
                    if nxt:
                        make_hi(nxt, D)
                    if far:
                        sum_squares(far)
                    if now:
                        copy_c(now, 1)
                    if nxt:
                        make_hi(nxt, A)
                        make_hi(nxt, B)
                    if far:
                        root(far)

                slots(p, act, emit)

            run(0)
            act.wait_ge(flag_ready, 1)
            with act.If(act.value_load(differ[0:1, 0:1], min_val=0, max_val=1) != 0):
                run(1)

        @block.vector
        def _(dve):
            nc.vector.memset(no_bias[:], 0.0).then_inc(pads_zeroed, 1)
            nc.vector.memset(parts[:].rearrange("p b j s r w -> p (b j s r) w")[:, :, 0:PW:PW - 1], 0.0).then_inc(pads_zeroed, 1)

            steps = [0]

            def step(ins):
                steps[0] += 1
                ins.then_inc(w_step, 1)
                dve.wait_ge(w_step, steps[0])

            dve.wait_ge(w_loaded, 16)
            raw = w_raw[:].rearrange("p c h w -> p (c h w)")
            nrm = w_norm[:].rearrange("p c h w -> p (c h w)")
            pos = w_pos[:].rearrange("p c h w -> p (c h w)")
            neg = w_neg[:].rearrange("p c h w -> p (c h w)")
            nc.vector.tensor_reduce(w_absmax[:], raw, AX_X, ALU.max, apply_absolute_value=True).then_inc(w_max_local, 1)
            dve.wait_ge(scalars_loaded, 48)
            nc.vector.tensor_tensor(differ[:], wp_sb[0:1, :], wn_sb[0:1, :], ALU.not_equal).then_inc(flag_ready, 1)
            nc.vector.tensor_scalar(out_scale[:, 0, 0:1], wp_sb[:], 1.0 / NORM_SCALE, None, ALU.mult)
            nc.vector.tensor_scalar(out_scale[:, 0, 1:2], wp_sb[:], -1.0 / NORM_SCALE, None, ALU.mult)
            nc.vector.tensor_scalar(out_scale[:, 1, 0:1], wn_sb[:], -1.0 / NORM_SCALE, None, ALU.mult)
            nc.vector.tensor_scalar(out_scale[:, 1, 1:2], wn_sb[:], 1.0 / NORM_SCALE, None, ALU.mult).then_inc(scale_ready, 1)
            nc.vector.tensor_tensor(equal[:], wp_sb[:], wn_sb[:], ALU.is_equal)
            dve.wait_ge(w_max_ready, 1)
            col = [w_consts[:, i:i + 1] for i in range(6)]
            step(nc.vector.tensor_scalar(col[0], w_max[:], 0.0, None, ALU.is_equal))
            step(nc.vector.tensor_tensor(col[1], w_max[:], col[0], ALU.add))
            step(nc.vector.reciprocal(col[2], col[1]))
            nc.vector.tensor_scalar(nrm, raw, col[2], None, ALU.mult)
            step(nc.vector.tensor_scalar(col[3], w_max[:], col[2], THRESHOLD, ALU.mult, ALU.mult))
            step(nc.vector.tensor_scalar(col[4], col[3], -1.0, None, ALU.mult))
            step(nc.vector.tensor_scalar(neg, nrm, col[4], equal[:], ALU.is_lt, ALU.mult))
            step(nc.vector.scalar_tensor_tensor(pos, nrm, col[3], neg, ALU.is_gt, ALU.subtract))
            nc.vector.tensor_scalar(neg, nrm, col[4], None, ALU.is_lt)

            def combine(p):
                w = [(w_neg if p else w_pos)[:, :, kh, :].rearrange("p c k -> p k c") for kh in range(TAPS)]
                wait(dve, w_turned, 4 * p)
                step(nc.vector.tensor_tensor(w_sum[:], w[0], w[2], ALU.add))
                step(nc.vector.tensor_scalar(w_sum[:], w_sum[:], 0.5, None, ALU.mult))
                step(nc.vector.tensor_scalar(w_mid[:], w[1], 0.5, None, ALU.mult))
                nc.vector.tensor_tensor(w_comb[:, C], w_sum[:], w_mid[:], ALU.add)
                nc.vector.tensor_tensor(w_comb[:, D], w_sum[:], w_mid[:], ALU.subtract)
                nc.vector.tensor_scalar(w_comb[:, A], w[0], 1.0, None, ALU.mult)
                nc.vector.tensor_scalar(w_comb[:, B], w[2], -1.0, None, ALU.mult).then_inc(w_comb_ready, 1)

            def run(p):
                def negate_mean(img):
                    dve.wait_ge(mean_summed, img.count(plus=1))
                    b = b_slice(img)
                    nc.vector.tensor_scalar(neg2mean[:, b], stat_ps[:, 0:1], 2.0, None, ALU.mult)
                    nc.vector.tensor_copy(negmean[:, b], stat_ps[:, 0:1]).then_inc(negmean_ready, 1)

                def edges(img):
                    dve.wait_ge(negmean_ready, img.count(plus=1))
                    for j in (A, B):
                        wait(dve, lo_ready[j], img.count(plus=-1))
                    xs, u, m = x_sb[img.buf], plane[img.pair], negmean[:, b_slice(img)]
                    nc.vector.tensor_scalar(u[A][:, 0, :], xs[:, 1, :], m, -1.0, ALU.add, ALU.mult)
                    nc.vector.tensor_scalar(u[B][:, PAIRS - 1, :], xs[:, H - 2, :], m, None,
                                            ALU.add).then_inc(edges_ready, 1)

                def sum_plane(img):
                    dve.wait_ge(negmean_ready, img.count(plus=1))
                    wait(dve, lo_ready[C], img.count(plus=-1))
                    xs = x_sb[img.buf]
                    nc.vector.scalar_tensor_tensor(plane[img.pair][C][:], xs[:, 0:H:2, :], neg2mean[:, b_slice(img)],
                                                   xs[:, 1:H:2, :], ALU.add, ALU.add).then_inc(plane_ready[C], 1)

                def variance(img):
                    dve.wait_ge(var_summed, img.count(plus=1))
                    nc.vector.tensor_scalar(var_eps[:, b_slice(img)], stat_ps[:, 1:2], -1.0, EPS,
                                            ALU.mult, ALU.add).then_inc(var_ready, 1)

                def scale_of_x(img):
                    b = b_slice(img)
                    dve.wait_ge(std_ready, img.count(plus=1))
                    nc.vector.reciprocal(rstd0[:, b], std[:, b]).then_inc(stat_step, 1)
                    dve.wait_ge(stat_step, img.count(3, 1))
                    nc.vector.tensor_scalar(newton[:, 0, b], rstd0[:, b], rstd0[:, b], var_eps[:, b],
                                            ALU.mult, ALU.mult).then_inc(stat_step, 1)
                    dve.wait_ge(stat_step, img.count(3, 2))
                    nc.vector.tensor_scalar(newton[:, 1, b], newton[:, 0, b], -0.5 * NORM_SCALE, 1.5 * NORM_SCALE,
                                            ALU.mult, ALU.add).then_inc(stat_step, 1)
                    dve.wait_ge(stat_step, img.count(3, 3))
                    nc.vector.tensor_tensor(norm_scale[:, b], rstd0[:, b], newton[:, 1, b],
                                            ALU.mult).then_inc(scale_of_x_ready, 1)

                def make_lo(img, j):
                    dve.wait_ge(hi_ready[j], img.count(plus=1))
                    nc.vector.scalar_tensor_tensor(part(img, j, LO), plane[img.pair][j][:], norm_scale[:, b_slice(img)],
                                                   part(img, j, HI), ALU.mult, ALU.subtract).then_inc(lo_ready[j], 1)

                def add_d(img, h):
                    dve.wait_ge(product_done, img.half(h, 4, D + 1))
                    for odd in range(2):
                        dve.wait_ge(residual_added, img.half(h, 2, odd + 1))
                        nc.vector.scalar_tensor_tensor(rows_sb[:, h, odd], product_ps(D), out_scale[:, p, odd:odd + 1],
                                                       rows_sb[:, h, odd], ALU.mult, ALU.add).then_inc(d_added, 1)

                def add_a_b(img, h):
                    for odd, prod, done in ((0, A, even_done), (1, B, odd_done)):
                        first = 2 * ROWS * h + odd
                        dve.wait_ge(product_done, img.half(h, 4, prod + 1))
                        dve.wait_ge(d_added, img.half(h, 2, odd + 1))
                        nc.vector.scalar_tensor_tensor(x_sb[img.buf][:, first:first + 2 * ROWS - 1:2, :],
                                                       product_ps(prod), out_scale[:, p, 0:1],
                                                       rows_sb[:, h, odd], ALU.mult, ALU.add).then_inc(done, 1)

                def emit(prev, now, nxt, far, ahead):
                    if prev:
                        add_a_b(prev, 1)
                    if nxt:
                        make_lo(nxt, C)
                    if now:
                        add_d(now, 0)
                    if far:
                        negate_mean(far)
                        edges(far)
                    if nxt:
                        make_lo(nxt, D)
                    if now:
                        add_a_b(now, 0)
                    if far:
                        sum_plane(far)
                        variance(far)
                    if nxt:
                        make_lo(nxt, A)
                        make_lo(nxt, B)
                    if far:
                        scale_of_x(far)
                    if now:
                        add_d(now, 1)

                slots(p, dve, emit)

            combine(0)
            run(0)
            with dve.If(dve.value_load(differ[0:1, 0:1], min_val=0, max_val=1) != 0):
                combine(1)
                run(1)

        @block.tensor
        def _(pe):
            def turn_weights(p):
                pe.wait_ge(consts_ready, 2)
                pe.wait_ge(w_comb_ready, p + 1)
                for s, per in ((c_ready, 1), (d_added, 2), (even_done, 1), (odd_done, 1)):
                    wait(pe, s, p * N_IMG * HALVES * per)
                for j in range(4):
                    for kw in range(TAPS):
                        ins = nc.tensor.matmul(product[j][:, kw * P:(kw + 1) * P], w_comb[:, j, kw, :], ident[:],
                                               start=True, stop=True)
                    ins.then_inc(w_turned, 1)

            def run(p):
                def sum_groups(img, of, ready, col, done):
                    pe.wait_ge(ready, img.count(plus=1))
                    wait(pe, var_ready, img.count())
                    nc.tensor.matmul(stat_ps[:, col:col + 1], group_mean[:], of[:, b_slice(img)],
                                     start=True, stop=True).then_inc(done, 1)

                def multiply(img, h, prod):
                    if h == 0:
                        pe.wait_ge(lo_ready[prod], img.count(plus=1))
                    for kw in range(TAPS):
                        for which in (HI, LO):
                            first, last = (kw, which) == (0, HI), (kw, which) == (TAPS - 1, LO)
                            for r0, r1 in ((0, ROWS0), (ROWS0, ROWS)):
                                ins = nc.tensor.matmul(product_ps(prod, r0, r1), w_lhsT[:, prod, kw, :],
                                                       parts[:, img.pair, prod, which, h * ROWS + r0:h * ROWS + r1, kw:kw + W],
                                                       start=first, stop=last)
                    ins.then_inc(product_done, 1)

                def emit(prev, now, nxt, far, ahead):
                    if now:
                        if nxt:
                            pe.wait_ge(var_ready, nxt.count(plus=1))
                        wait(pe, c_ready, now.half(0))
                        multiply(now, 0, C)
                        wait(pe, d_added, now.half(0, 2))
                        multiply(now, 0, D)
                        wait(pe, even_done, now.half(0))
                        multiply(now, 0, A)
                        pe.wait_ge(c_ready, now.half(0, 1, 1))
                    if far:
                        sum_groups(far, x_sum, sum_ready, 0, mean_summed)
                    if now:
                        wait(pe, odd_done, now.half(0))
                        multiply(now, 0, B)
                        if far:
                            pe.wait_ge(negmean_ready, far.count(plus=1))
                        multiply(now, 1, C)
                        pe.wait_ge(d_added, now.half(1, 2))
                        multiply(now, 1, D)
                        pe.wait_ge(c_ready, now.half(1, 1, 1))
                    if far:
                        sum_groups(far, x_sumsq, sumsq_ready, 1, var_summed)
                    if now:
                        pe.wait_ge(even_done, now.half(1))
                        multiply(now, 1, A)
                        pe.wait_ge(odd_done, now.half(1))
                        multiply(now, 1, B)

                slots(p, pe, emit)

            turn_weights(0)
            pe.wait_ge(w_ready, 4)
            pe.wait_ge(pads_zeroed, 2)
            run(0)
            pe.wait_ge(flag_ready, 1)
            with pe.If(pe.value_load(differ[0:1, 0:1], min_val=0, max_val=1) != 0):
                turn_weights(1)
                pe.wait_ge(w_ready, 8)
                run(1)


_INS = ['x', 'L0_conv_weight', 'L0_conv_bias', 'L0_conv_Wp', 'L0_conv_Wn']


def kernel(**inputs):
    import numpy as _np
    import concourse.bacc as _bacc
    from concourse import mybir as _mybir
    from concourse.bass_utils import run_bass_kernel_spmd as _run

    nc = _bacc.Bacc("TRN2", target_bir_lowering=False, num_devices=1)
    arrays, args = {}, []
    for name in _INS:
        a = _np.ascontiguousarray(inputs[name])
        arrays[f"in_{name}_dram"] = a
        args.append(nc.dram_tensor(f"in_{name}_dram", a.shape, _mybir.dt.from_np(a.dtype), kind="ExternalInput").ap())
    shape = inputs['x'].shape
    args.append(nc.dram_tensor("out_0_dram", shape, _mybir.dt.float32, kind="ExternalOutput").ap())
    conv_preact_kernel(nc, *args)
    r = _run(nc, [arrays], core_ids=[0])
    return r.results[0]["out_0_dram"]
```

```python
from contextlib import ExitStack

import concourse.bass as bass
from concourse import mybir


P = 128
GROUPS = 32
EPS = 1e-5
THRESHOLD = 0.05
NORM_SCALE = 256.0
X_BUFS = 4
HALVES = 2
C, D, A, B = range(4)
EVEN, ODD = range(2)
CUTS = (2, 1, 1, 1)
HI, LO = range(2)
PSUM_BANK = 512
WARM_UP = 11

ALU = mybir.AluOpType
ACT = mybir.ActivationFunctionType
F16 = mybir.dt.float16
F32 = mybir.dt.float32
I32 = mybir.dt.int32
AX_X = mybir.AxisListType.X


def conv_preact_kernel(nc, x, weight, bias, wp, wn, out):
    N_IMG, CH, H, W = x.shape
    TAPS = 3
    PAIRS = H // 2
    ROWS = PAIRS // HALVES
    COLS = ROWS * W
    ROWS0 = PSUM_BANK // W
    GROUP_N = CH // GROUPS * H * W
    assert CH == P and weight.shape == (P, P, TAPS, TAPS) and PAIRS % HALVES == 0
    assert N_IMG % X_BUFS == 0 and N_IMG >= 2 * X_BUFS
    assert ROWS0 < ROWS and (ROWS - ROWS0) * W < PSUM_BANK - 2

    x_dram = x.rearrange("n c h w -> n c (h w)")
    out_dram = out.rearrange("n c h w -> n c (h w)")

    with ExitStack() as ctx:
        def sb(name, shape, dt=F32):
            return ctx.enter_context(nc.sbuf_tensor(name, shape, dt))

        def sem(name):
            return ctx.enter_context(nc.semaphore(name))

        x_sb = [sb(f"x{b}", [P, H, W]) for b in range(X_BUFS)]
        plane = [[sb(f"plane{b}_{j}", [P, PAIRS, W]) for j in range(4)] for b in range(2)]
        parts = sb("parts", [P, 2, 4, 2, PAIRS, W], F16)
        c_sb = sb("c_sb", [P, HALVES, ROWS, W])
        d_sb = sb("d_sb", [P, HALVES, ROWS, W])
        y_sb = [sb(f"y{b}", [P, H, W]) for b in range(2)]
        junk = sb("junk", [P, H * W], F16)
        w_raw = y_sb[1][:].rearrange("p h w -> p (h w)")[:, 0:P * TAPS * TAPS]
        w_pos = sb("w_pos", [P, P, TAPS, TAPS], F16)
        w_neg = sb("w_neg", [P, P, TAPS, TAPS], F16)
        w_sum = sb("w_sum", [P, TAPS, P], F16)
        w_mid = sb("w_mid", [P, TAPS, P], F16)
        w_comb = sb("w_comb", [P, 4, TAPS, P], F16)
        w_lhsT = sb("w_lhsT", [P, 4, TAPS, P], F16)
        ident = sb("ident", [P, P], F16)
        group_mean = sb("group_mean", [P, P])
        w_absmax = sb("w_absmax", [P, 1])
        w_max = sb("w_max", [P, 1])
        w_consts = sb("w_consts", [P, 8])
        bias_sb = sb("bias_sb", [P, 1])
        wp_sb = sb("wp_sb", [P, 1])
        wn_sb = sb("wn_sb", [P, 1])
        equal = sb("equal", [P, 1])
        differ = sb("differ", [1, 1], I32)
        no_bias = sb("no_bias", [P, 1])
        root_of_zero = sb("root_of_zero", [P, 1])
        out_scale = sb("out_scale", [P, 2, 2])
        sums = sb("sums", [P, X_BUFS, 2])
        negmean = sb("negmean", [P, X_BUFS])
        neg2mean = sb("neg2mean", [P, X_BUFS])
        mean = sb("mean", [P, X_BUFS])
        var_eps = sb("var_eps", [P, X_BUFS])
        std = sb("std", [P, X_BUFS])
        rstd0 = sb("rstd0", [P, X_BUFS])
        newton = sb("newton", [P, X_BUFS])
        norm_scale = sb("norm_scale", [P, X_BUFS])

        rows_ps = [[ctx.enter_context(nc.psum_tensor(f"{name}_rows{h}", [P, 2 * PSUM_BANK], F32))
                    for name in ("even", "odd")] for h in range(HALVES)]
        FIRST_COL = PSUM_BANK - ROWS0 * W
        var_ps = rows_ps[0][EVEN][:, 2 * PSUM_BANK - 2:2 * PSUM_BANK - 1]
        mean_ps = rows_ps[0][EVEN][:, 2 * PSUM_BANK - 1:2 * PSUM_BANK]
        first_mean_ps = rows_ps[1][ODD][:, 2 * PSUM_BANK - 1:2 * PSUM_BANK]

        def product_ps(h, odd, r0=0, r1=ROWS):
            return rows_ps[h][odd][:, FIRST_COL + r0 * W:FIRST_COL + r1 * W].rearrange("p (r w) -> p r w", w=W)

        x_loaded = [sem(f"x_loaded{b}") for b in range(X_BUFS)]
        prev_loaded = [sem(f"prev_loaded{b}") for b in range(X_BUFS)]
        residual_added = [[sem(f"residual_added{b}_{h}") for h in range(HALVES)] for b in range(2)]
        y_stored = [[sem(f"y_stored{b}_{h}") for h in range(HALVES)] for b in range(2)]
        w_loaded = sem("w_loaded")
        scalars_loaded = sem("scalars_loaded")
        consts_step = sem("consts_step")
        consts_ready = sem("consts_ready")
        w_max_local = sem("w_max_local")
        w_max_ready = sem("w_max_ready")
        w_step = sem("w_step")
        flag_ready = sem("flag_ready")
        scale_ready = sem("scale_ready")
        zero_ready = sem("zero_ready")
        w_comb_ready = sem("w_comb_ready")
        w_turned = sem("w_turned")
        w_ready = sem("w_ready")
        sum_ready = sem("sum_ready")
        first_mean_summed = sem("first_mean_summed")
        negmean_ready = sem("negmean_ready")
        sumsq_ready = sem("sumsq_ready")
        summed = sem("summed")
        var_ready = sem("var_ready")
        std_ready = sem("std_ready")
        rstd_ready = sem("rstd_ready")
        newton_ready = sem("newton_ready")
        scale_of_x_ready = sem("scale_of_x_ready")
        edges_ready = sem("edges_ready")
        plane_ready = [sem(f"plane_ready{j}") for j in range(4)]
        hi_ready = [sem(f"hi_ready{j}") for j in range(4)]
        lo_ready = [sem(f"lo_ready{j}") for j in range(4)]
        product_done = [sem(f"product_done{j}") for j in range(4)]
        c_ready = sem("c_ready")
        d_ready = sem("d_ready")
        even_done = sem("even_done")
        last_residual = sem("last_residual")
        odd_done = sem("odd_done")

        def wait(eng, s, value):
            if not (isinstance(value, int) and value <= 0):
                eng.wait_ge(s, value)

        class Image:

            def __init__(self, q, j):
                self.buf = j % X_BUFS
                self.turn = q + j // X_BUFS
                self.pair = j % 2
                self.q, self.j = q, j

            def count(self, per=1, plus=0):
                return self.q * (per * X_BUFS) + (self.j * per + plus)

            def pair_turns(self, per, plus=0):
                return self.q * (per * X_BUFS // 2) + (self.j // 2 * per + plus)

            def half(self, h, per=1, plus=0):
                return self.count(HALVES * per, h * per + plus)

        def slots(p, eng, emit):
            q0 = p * N_IMG // X_BUFS

            def edge_slot(k):
                emit(*[Image(q0, k + d) if 0 <= k + d < N_IMG else None for d in range(-1, 3)])

            for k in range(-1, 2):
                edge_slot(k)
            with eng.Fori(q0, q0 + N_IMG // X_BUFS - 1) as q:
                for j in range(2, X_BUFS + 2):
                    emit(*[Image(q, j + d) for d in range(-1, 3)])
            for k in range(N_IMG - X_BUFS + 2, N_IMG + 1):
                edge_slot(k)

        def turned_ps(j):
            return rows_ps[j // 2][j % 2][:, 0:TAPS * P]

        def b_slice(img):
            return slice(img.buf, img.buf + 1)

        def piece(t, j, i):
            n = PAIRS // CUTS[j]
            return t[:, i * n:(i + 1) * n, :]

        def part(img, j, which):
            return parts[:, img.pair, j, which]

        def used(img, j):
            return img.count(CUTS[j], -CUTS[j])

        block = ctx.enter_context(nc.Block())

        @block.sync
        def _(sp):
            sp.dma_start(w_raw, weight.rearrange("o i h w -> o (i h w)")).then_inc(w_loaded, 16)
            sp.dma_start(bias_sb[:], bias.rearrange("(c a) -> c a", a=1)).then_inc(scalars_loaded, 16)
            sp.dma_start(wp_sb[:], wp.rearrange("(a b) -> a b", a=1).broadcast_to([P, 1])).then_inc(scalars_loaded, 16)
            sp.dma_start(wn_sb[:], wn.rearrange("(a b) -> a b", a=1).broadcast_to([P, 1])).then_inc(scalars_loaded, 16)

            def run(p):
                def half_of(t, h):
                    return t[:, 2 * ROWS * h:2 * ROWS * (h + 1), :].rearrange("p h w -> p (h w)")

                def in_dram(t, img, h):
                    return t[img.count(plus=-p * N_IMG)][:, h * 2 * COLS:(h + 1) * 2 * COLS]

                def residuals(img, plus):
                    return img.pair_turns(16, plus - 16 * p * (img.pair == (N_IMG - 1) % 2))

                def load(img, h):
                    wait(sp, residual_added[img.pair][h], residuals(img, 16 - 16 * (X_BUFS // 2)))
                    sp.dma_start(half_of(x_sb[img.buf], h), in_dram(x_dram, img, h)).then_inc(x_loaded[img.buf], 16)

                def store(img, h, last):
                    if last:
                        sp.wait_ge(even_done, img.half(h, 1, 1))
                        sp.wait_ge(odd_done, img.half(h, 1, 1))
                    else:
                        sp.wait_ge(residual_added[img.pair][h], residuals(img, 16))
                    sp.dma_start(in_dram(out_dram, img, h), half_of(y_sb[img.pair], h)).then_inc(y_stored[img.pair][h], 16)

                def load_first_output(img):
                    for s in plane_ready + [edges_ready, sumsq_ready]:
                        sp.wait_ge(s, img.count(plus=1))
                    for h in range(HALVES):
                        sp.dma_start(half_of(x_sb[img.buf], h), in_dram(out_dram, img, h)).then_inc(prev_loaded[img.buf], 16)

                def emit(prev, now, nxt, far):
                    if nxt and not now:
                        load(nxt, 0)
                        load(nxt, 1)
                    if far:
                        load(far, 0)
                        load(far, 1)
                    if prev:
                        store(prev, 0, last=not now)
                        store(prev, 1, last=not now)
                    if p and nxt:
                        load_first_output(nxt)

                slots(p, sp, emit)
                for b in range(2):
                    for h in range(HALVES):
                        sp.wait_ge(y_stored[b][h], (p + 1) * N_IMG // 2 * 16)

            run(0)
            sp.wait_ge(flag_ready, 1)
            with sp.If(sp.value_load(differ[0:1, 0:1], min_val=0, max_val=1) != 0):
                run(1)

        @block.gpsimd
        def _(pool):
            nc.gpsimd.memset(group_mean[:], -1.0 / GROUP_N).then_inc(consts_step, 1)
            nc.gpsimd.memset(ident[:], 0.0).then_inc(consts_step, 1)
            pool.wait_ge(consts_step, 2)
            per = P // GROUPS
            g = group_mean[:].rearrange("p (g c) -> p g c", c=per)
            nc.gpsimd.affine_select(out=g, in_=g, compare_op=ALU.is_ge, fill=0.0, base=0,
                                    pattern=[[-per, GROUPS], [0, per]], channel_multiplier=1).then_inc(consts_step, 1)
            nc.gpsimd.affine_select(out=ident[:], in_=ident[:], compare_op=ALU.not_equal, fill=1.0, base=0,
                                    pattern=[[-1, P]], channel_multiplier=1).then_inc(consts_ready, 1)
            pool.wait_ge(consts_step, 3)
            nc.gpsimd.affine_select(out=g, in_=g, compare_op=ALU.is_ge, fill=0.0, base=per - 1,
                                    pattern=[[per, GROUPS], [0, per]], channel_multiplier=-1).then_inc(consts_ready, 1)
            pool.wait_ge(w_max_local, 1)
            nc.gpsimd.partition_all_reduce(w_max[:], w_absmax[:], P, bass.bass_isa.ReduceOp.max).then_inc(w_max_ready, 1)

            def run(p):
                def difference(img, j):
                    pool.wait_ge(x_loaded[img.buf], img.turn * 32 + 32)
                    wait(pool, lo_ready[j], used(img, j))
                    xs, u = x_sb[img.buf], plane[img.pair][j]
                    even, odd = xs[:, 0:H:2, :], xs[:, 1:H:2, :]
                    o, a, b = {D: (u[:], odd, even),
                               A: (u[:, 1:, :], odd[:, 0:PAIRS - 1, :], odd[:, 1:, :]),
                               B: (u[:, 0:PAIRS - 1, :], even[:, 0:PAIRS - 1, :], even[:, 1:, :])}[j]
                    nc.gpsimd.tensor_tensor(o, a, b, ALU.subtract).then_inc(plane_ready[j], 1)

                def add_residual(img, h):
                    written = img.half(h, 1, 1)
                    loaded = (img.turn - N_IMG // X_BUFS) * 32 + 32
                    if not isinstance(written, int):
                        written, loaded = pool.to_reg(written), pool.to_reg(loaded)
                    pool.wait_ge(consts_ready, 2)
                    pool.wait_ge(even_done, written)
                    pool.wait_ge(odd_done, written)
                    if p:
                        pool.wait_ge(prev_loaded[img.buf], loaded)
                    y, r = (t[:, 2 * ROWS * h:2 * ROWS * (h + 1), :].rearrange("p h w -> p (h w)")
                            for t in (y_sb[img.pair], x_sb[img.buf]))
                    pool.dma_start(y, r, accum_op=ALU.add).then_inc(residual_added[img.pair][h], 16)

                def add_last_residual(img, h):
                    if p:
                        pool.wait_ge(prev_loaded[img.buf], (img.turn - N_IMG // X_BUFS) * 32 + 32)
                    for odd, t, ready in ((1, c_sb, c_ready), (0, d_sb, d_ready)):
                        pool.wait_ge(ready, img.half(h, 1, 1))
                        first = 2 * ROWS * h + odd
                        nc.gpsimd.tensor_tensor(t[:, h], t[:, h], x_sb[img.buf][:, first:first + 2 * ROWS - 1:2, :],
                                                ALU.add).then_inc(last_residual, 1)

                def emit(prev, now, nxt, far):
                    if now and not nxt:
                        add_residual(prev, 1)
                        add_last_residual(now, 0)
                        add_last_residual(now, 1)
                    elif prev and now:
                        add_residual(prev, 1)
                    if nxt:
                        difference(nxt, D)
                        difference(nxt, A)
                        difference(nxt, B)
                    if now and nxt:
                        add_residual(now, 0)

                slots(p, pool, emit)

            run(0)
            pool.wait_ge(flag_ready, 1)
            with pool.If(pool.value_load(differ[0:1, 0:1], min_val=0, max_val=1) != 0):
                run(1)

        @block.scalar
        def _(act):
            act.wait_ge(zero_ready, 1)
            nc.scalar.activation(root_of_zero[:], no_bias[:], ACT.Sqrt)

            def run(p):
                def copy_c(img, h):
                    if p == 0:
                        act.wait_ge(scale_ready, 1)
                        act.wait_ge(scalars_loaded, 48)
                    act.wait_ge(product_done[C], img.half(h, 1, 1))
                    wait(act, odd_done, img.half(h, 1, -1))
                    nc.scalar.activation(c_sb[:, h], product_ps(h, EVEN), ACT.Identity,
                                         bias=(no_bias if p else bias_sb)[:, 0:1],
                                         scale=out_scale[:, p, 0:1]).then_inc(c_ready, 1)

                def make_hi(img, j):
                    act.wait_ge(scale_of_x_ready, img.count(plus=1))
                    act.wait_ge(plane_ready[j], img.count(plus=1))
                    if j in (A, B):
                        act.wait_ge(edges_ready, img.count(plus=1))
                    wait(act, product_done[j], img.count(HALVES, -HALVES))
                    for i in range(CUTS[j]):
                        nc.scalar.activation(piece(part(img, j, HI), j, i), piece(plane[img.pair][j], j, i), ACT.Copy,
                                             scale=norm_scale[:, b_slice(img)]).then_inc(hi_ready[j], 1)

                def sum_x(img):
                    act.wait_ge(x_loaded[img.buf], img.turn * 32 + 32)
                    wait(act, sumsq_ready, img.count())
                    nc.scalar.activation(junk[:], x_sb[img.buf][:].rearrange("p h w -> p (h w)"), ACT.Copy,
                                         accum_out=sums[:, (img.buf - 1) % X_BUFS, 1:2]).then_inc(sum_ready, 1)

                def take_mean(img, first):
                    if first:
                        act.wait_ge(first_mean_summed, 2 * p + img.j + 1)
                    else:
                        act.wait_ge(summed, img.count())
                        act.wait_ge(var_ready, img.count())
                    b, ps = b_slice(img), first_mean_ps if first else mean_ps
                    nc.scalar.activation(neg2mean[:, b], ps, ACT.Copy, scale=2.0)
                    nc.scalar.activation(mean[:, b], ps, ACT.Copy, scale=-1.0)
                    nc.scalar.activation(negmean[:, b], ps, ACT.Copy).then_inc(negmean_ready, 1)

                def edges(img):
                    act.wait_ge(negmean_ready, img.count(plus=1))
                    b = b_slice(img)
                    for j in (A, B):
                        wait(act, lo_ready[j], used(img, j))
                    xs, u = x_sb[img.buf], plane[img.pair]
                    nc.scalar.activation(u[A][:, 0, :], xs[:, 1, :], ACT.Identity, bias=mean[:, b], scale=-1.0)
                    nc.scalar.activation(u[B][:, PAIRS - 1, :], xs[:, H - 2, :], ACT.Identity,
                                         bias=negmean[:, b]).then_inc(edges_ready, 1)

                def sum_squares(img):
                    act.wait_ge(negmean_ready, img.count(plus=1))
                    act.wait_ge(sum_ready, img.count(plus=1))
                    nc.scalar.activation(junk[:], x_sb[img.buf][:].rearrange("p h w -> p (h w)"), ACT.Square,
                                         bias=negmean[:, b_slice(img)],
                                         accum_out=sums[:, img.buf, 0:1]).then_inc(sumsq_ready, 1)

                def root(img):
                    act.wait_ge(var_ready, img.count(plus=1))
                    nc.scalar.activation(std[:, b_slice(img)], var_eps[:, b_slice(img)], ACT.Sqrt).then_inc(std_ready, 1)

                def emit(prev, now, nxt, far):
                    first_slot, second_slot = not now and not prev, now and not prev
                    if now:
                        make_hi(now, A)
                    if first_slot:
                        sum_x(nxt)
                    if now:
                        make_hi(now, B)
                    if second_slot:
                        copy_c(now, 0)
                    if first_slot or second_slot:
                        take_mean(nxt, True)
                    if first_slot:
                        sum_squares(nxt)
                        edges(nxt)
                    elif nxt:
                        edges(nxt)
                    if now and not second_slot:
                        copy_c(now, 0)
                    if now and nxt:
                        sum_squares(nxt)
                    if now:
                        if far:
                            sum_x(far)
                        copy_c(now, 1)
                    if nxt:
                        root(nxt)
                    if now and far:
                        take_mean(far, False)
                    if nxt:
                        make_hi(nxt, C)
                        make_hi(nxt, D)
                slots(p, act, emit)

            run(0)
            act.wait_ge(flag_ready, 1)
            with act.If(act.value_load(differ[0:1, 0:1], min_val=0, max_val=1) != 0):
                run(1)

        @block.vector
        def _(dve):
            nc.vector.memset(no_bias[:], 0.0).then_inc(zero_ready, 1)

            steps = [0]

            def step(ins):
                steps[0] += 1
                ins.then_inc(w_step, 1)
                dve.wait_ge(w_step, steps[0])

            dve.wait_ge(w_loaded, 16)
            pos = w_pos[:].rearrange("p c h w -> p (c h w)")
            neg = w_neg[:].rearrange("p c h w -> p (c h w)")
            nc.vector.tensor_reduce(w_absmax[:], w_raw, AX_X, ALU.max, apply_absolute_value=True).then_inc(w_max_local, 1)
            dve.wait_ge(scalars_loaded, 48)
            nc.vector.tensor_tensor(differ[:], wp_sb[0:1, :], wn_sb[0:1, :], ALU.not_equal).then_inc(flag_ready, 1)
            nc.vector.tensor_scalar(out_scale[:, 0, 0:1], wp_sb[:], 1.0 / NORM_SCALE, None, ALU.mult)
            nc.vector.tensor_scalar(out_scale[:, 0, 1:2], wp_sb[:], -1.0 / NORM_SCALE, None, ALU.mult)
            nc.vector.tensor_scalar(out_scale[:, 1, 0:1], wn_sb[:], -1.0 / NORM_SCALE, None, ALU.mult)
            nc.vector.tensor_scalar(out_scale[:, 1, 1:2], wn_sb[:], 1.0 / NORM_SCALE, None, ALU.mult).then_inc(scale_ready, 1)
            nc.vector.tensor_tensor(equal[:], wp_sb[:], wn_sb[:], ALU.is_equal)
            dve.wait_ge(w_max_ready, 1)
            col = [w_consts[:, i:i + 1] for i in range(6)]
            step(nc.vector.tensor_scalar(col[0], w_max[:], 0.0, None, ALU.is_equal))
            step(nc.vector.tensor_tensor(col[1], w_max[:], col[0], ALU.add))
            step(nc.vector.reciprocal(col[2], col[1]))
            nc.vector.tensor_scalar(w_raw, w_raw, col[2], None, ALU.mult)
            step(nc.vector.tensor_scalar(col[3], w_max[:], col[2], THRESHOLD, ALU.mult, ALU.mult))
            step(nc.vector.tensor_scalar(col[4], col[3], -1.0, None, ALU.mult))
            step(nc.vector.tensor_scalar(neg, w_raw, col[4], equal[:], ALU.is_lt, ALU.mult))
            step(nc.vector.scalar_tensor_tensor(pos, w_raw, col[3], neg, ALU.is_gt, ALU.subtract))
            nc.vector.tensor_scalar(neg, w_raw, col[4], None, ALU.is_lt)

            def combine(p):
                w = [(w_neg if p else w_pos)[:, :, kh, :].rearrange("p c k -> p k c") for kh in range(TAPS)]
                wait(dve, w_turned, 4 * p)
                step(nc.vector.tensor_tensor(w_sum[:], w[0], w[2], ALU.add))
                step(nc.vector.tensor_scalar(w_sum[:], w_sum[:], 0.5, None, ALU.mult))
                step(nc.vector.tensor_scalar(w_mid[:], w[1], 0.5, None, ALU.mult))
                nc.vector.tensor_tensor(w_comb[:, C], w_sum[:], w_mid[:], ALU.add)
                nc.vector.tensor_tensor(w_comb[:, D], w_mid[:], w_sum[:], ALU.subtract)
                nc.vector.tensor_scalar(w_comb[:, A], w[0], 1.0, None, ALU.mult)
                nc.vector.tensor_scalar(w_comb[:, B], w[2], -1.0, None, ALU.mult).then_inc(w_comb_ready, 1)

            def run(p):
                def turned_weights(js):
                    for j in js:
                        wait(dve, product_done[j], p * N_IMG * HALVES)
                        dve.wait_ge(w_turned, 4 * p + j + 1)
                        nc.vector.tensor_copy(w_lhsT[:, j].rearrange("p k c -> p (k c)"), turned_ps(j)).then_inc(w_ready, 1)

                def sum_plane(img):
                    dve.wait_ge(negmean_ready, img.count(plus=1))
                    wait(dve, lo_ready[C], used(img, C))
                    xs = x_sb[img.buf]
                    nc.vector.scalar_tensor_tensor(plane[img.pair][C][:], xs[:, 0:H:2, :], neg2mean[:, b_slice(img)],
                                                   xs[:, 1:H:2, :], ALU.add, ALU.add).then_inc(plane_ready[C], 1)

                def variance(img):
                    dve.wait_ge(summed, img.count(plus=1))
                    by = (NORM_SCALE / 2) ** -2
                    nc.vector.tensor_scalar(var_eps[:, b_slice(img)], var_ps, -by, EPS * by,
                                            ALU.mult, ALU.add).then_inc(var_ready, 1)

                def first_rstd(img):
                    b = b_slice(img)
                    dve.wait_ge(std_ready, img.count(plus=1))
                    nc.vector.reciprocal(rstd0[:, b], std[:, b]).then_inc(rstd_ready, 1)

                def newton_factor(img):
                    b = b_slice(img)
                    dve.wait_ge(rstd_ready, img.count(plus=1))
                    nc.vector.scalar_tensor_tensor(newton[:, b], rstd0[:, b], var_eps[:, b], rstd0[:, b],
                                                   ALU.mult, ALU.mult).then_inc(newton_ready, 1)

                def scale_of_x(img):
                    b = b_slice(img)
                    dve.wait_ge(newton_ready, img.count(plus=1))
                    nc.vector.scalar_tensor_tensor(norm_scale[:, b], newton[:, b], 3.0, rstd0[:, b], ALU.subtract,
                                                   ALU.mult, reverse0=True).then_inc(scale_of_x_ready, 1)

                def make_lo(img, j):
                    for i in range(CUTS[j]):
                        dve.wait_ge(hi_ready[j], img.count(CUTS[j], i + 1))
                        nc.vector.scalar_tensor_tensor(piece(part(img, j, LO), j, i), piece(plane[img.pair][j], j, i),
                                                       norm_scale[:, b_slice(img)], piece(part(img, j, HI), j, i),
                                                       ALU.mult, ALU.subtract).then_inc(lo_ready[j], 1)

                def y_rows(img, h, odd):
                    first = 2 * ROWS * h + odd
                    return y_sb[img.pair][:, first:first + 2 * ROWS - 1:2, :]

                def sum_second_x(img):
                    dve.wait_ge(x_loaded[img.buf], img.turn * 32 + 32)
                    nc.vector.tensor_reduce(sums[:, (img.buf - 1) % X_BUFS, 1:2], x_sb[img.buf][:].rearrange("p h w -> p (h w)"),
                                            AX_X, ALU.add).then_inc(sum_ready, 1)

                def copy_d(img, h):
                    dve.wait_ge(product_done[D], img.half(h, 1, 1))
                    wait(dve, even_done, img.half(h, 1, -1))
                    nc.vector.tensor_scalar(d_sb[:, h], product_ps(h, ODD), out_scale[:, p, 1:2],
                                            (no_bias if p else bias_sb)[:, 0:1], ALU.mult, ALU.add).then_inc(d_ready, 1)

                def output_rows(img, h, odd, last=False):
                    prod, other, ready, done = ((A, d_sb, d_ready, even_done), (B, c_sb, c_ready, odd_done))[odd]
                    dve.wait_ge(product_done[prod], img.half(h, 1, 1))
                    dve.wait_ge(ready, img.half(h, 1, 1))
                    if last:
                        dve.wait_ge(last_residual, 2 * HALVES * p + 2 * h + (1 if odd else 2))
                    wait(dve, y_stored[img.pair][h], img.pair_turns(16))
                    nc.vector.scalar_tensor_tensor(y_rows(img, h, odd), product_ps(h, odd), out_scale[:, p, 0:1],
                                                   other[:, h], ALU.mult, ALU.add).then_inc(done, 1)

                def emit(prev, now, nxt, far):
                    first_slot = not now and not prev
                    if prev:
                        output_rows(prev, 1, ODD, last=not now)
                    if now:
                        make_lo(now, A)
                        copy_d(now, 0)
                        make_lo(now, B)
                        output_rows(now, 0, EVEN, last=not nxt)
                    if nxt:
                        sum_plane(nxt)
                        if first_slot:
                            turned_weights((0, 1))
                        variance(nxt)
                        first_rstd(nxt)
                        newton_factor(nxt)
                        scale_of_x(nxt)
                        if first_slot:
                            turned_weights((2, 3))
                    if now:
                        copy_d(now, 1)
                        output_rows(now, 0, ODD, last=not nxt)
                    if nxt:
                        make_lo(nxt, C)
                        make_lo(nxt, D)
                    if first_slot:
                        sum_second_x(far)
                    if now:
                        output_rows(now, 1, EVEN, last=not nxt)

                slots(p, dve, emit)

            combine(0)
            run(0)
            with dve.If(dve.value_load(differ[0:1, 0:1], min_val=0, max_val=1) != 0):
                combine(1)
                run(1)

        @block.tensor
        def _(pe):
            def run(p):
                def turn_weights():
                    pe.wait_ge(w_comb_ready, p + 1)
                    for j in range(4):
                        for kw in range(TAPS):
                            ins = nc.tensor.matmul(turned_ps(j)[:, kw * P:(kw + 1) * P], w_comb[:, j, kw, :], ident[:],
                                                   start=True, stop=True)
                        ins.then_inc(w_turned, 1)

                def warm_up():
                    for _ in range(WARM_UP):
                        nc.tensor.matmul(rows_ps[1][EVEN][:, PSUM_BANK:PSUM_BANK + TAPS * P], ident[:],
                                         w_comb[:, C].rearrange("p k c -> p (k c)"), start=True, stop=True)

                def sum_first_mean(img):
                    pe.wait_ge(sum_ready, img.count(plus=1))
                    wait(pe, negmean_ready, img.count())
                    nc.tensor.matmul(first_mean_ps, group_mean[:], sums[:, (img.buf - 1) % X_BUFS, 1:2],
                                     start=True, stop=True).then_inc(first_mean_summed, 1)

                def sum_groups(img, after):
                    pe.wait_ge(sumsq_ready, img.count(plus=1))
                    wait(pe, var_ready, img.count())
                    if after:
                        pe.wait_ge(sum_ready, after.count(plus=1))
                        pe.wait_ge(negmean_ready, after.count())
                    n = 2 if after else 1
                    nc.tensor.matmul(rows_ps[0][EVEN][:, 2 * PSUM_BANK - 2:2 * PSUM_BANK - 2 + n], group_mean[:],
                                     sums[:, img.buf, 0:n], start=True, stop=True).then_inc(summed, 1)

                def multiply(img, h, prod):
                    if h < CUTS[prod]:
                        pe.wait_ge(lo_ready[prod], img.count(CUTS[prod], h + 1))
                    if prod in (C, D):
                        wait(pe, {C: even_done, D: odd_done}[prod], img.half(h, 1, -1))
                    else:
                        pe.wait_ge({A: c_ready, B: d_ready}[prod], img.half(h, 1, 1))
                    odd = prod in (D, B)
                    for kw, which in ((1, HI), (0, HI), (0, LO), (2, HI), (2, LO), (1, LO)):
                        to, of = max(1 - kw, 0), max(kw - 1, 0)
                        n = W - abs(kw - 1)
                        for r0, r1 in ((0, ROWS0), (ROWS0, ROWS)):
                            ins = nc.tensor.matmul(product_ps(h, odd, r0, r1)[:, :, to:to + n], w_lhsT[:, prod, kw, :],
                                                   parts[:, img.pair, prod, which, h * ROWS + r0:h * ROWS + r1, of:of + n],
                                                   start=(kw, which) == (1, HI) and prod in (C, D),
                                                   stop=(kw, which) == (1, LO),
                                                   skip_group_check=prod in (A, B))
                    ins.then_inc(product_done[prod], 1)

                def emit(prev, now, nxt, far):
                    first_slot, second_slot = not now and not prev, now and not prev
                    if first_slot:
                        wait(pe, odd_done, nxt.half(0))
                        wait(pe, even_done, nxt.half(0))
                        sum_first_mean(nxt)
                        turn_weights()
                        sum_groups(nxt, None)
                        warm_up()
                    if second_slot:
                        pe.wait_ge(w_ready, 4 * p + 4)
                    if now:
                        pe.wait_ge(var_ready, now.count(plus=1))
                        if prev and nxt:
                            pe.wait_ge(negmean_ready, nxt.count(plus=1))
                        multiply(now, 0, C)
                        multiply(now, 0, D)
                        if second_slot:
                            sum_first_mean(nxt)
                        multiply(now, 1, C)
                        multiply(now, 0, A)
                        if second_slot:
                            pe.wait_ge(negmean_ready, nxt.count(plus=1))
                        multiply(now, 1, D)
                        if second_slot:
                            multiply(now, 0, B)
                        if nxt:
                            pe.wait_ge(even_done, now.half(0, 1, 1))
                            sum_groups(nxt, far)
                        if not second_slot:
                            multiply(now, 0, B)
                        multiply(now, 1, A)
                        multiply(now, 1, B)

                slots(p, pe, emit)

            pe.wait_ge(consts_ready, 2)
            run(0)
            pe.wait_ge(flag_ready, 1)
            with pe.If(pe.value_load(differ[0:1, 0:1], min_val=0, max_val=1) != 0):
                run(1)


_INS = ['x', 'L0_conv_weight', 'L0_conv_bias', 'L0_conv_Wp', 'L0_conv_Wn']


def kernel(**inputs):
    import numpy as _np
    import concourse.bacc as _bacc
    from concourse import mybir as _mybir
    from concourse.bass_utils import run_bass_kernel_spmd as _run

    nc = _bacc.Bacc("TRN2", target_bir_lowering=False, num_devices=1)
    arrays, args = {}, []
    for name in _INS:
        a = _np.ascontiguousarray(inputs[name])
        arrays[f"in_{name}_dram"] = a
        args.append(nc.dram_tensor(f"in_{name}_dram", a.shape, _mybir.dt.from_np(a.dtype), kind="ExternalInput").ap())
    shape = inputs['x'].shape
    args.append(nc.dram_tensor("out_0_dram", shape, _mybir.dt.float32, kind="ExternalOutput").ap())
    conv_preact_kernel(nc, *args)
    r = _run(nc, [arrays], core_ids=[0])
    return r.results[0]["out_0_dram"]
```
